# Optimizing a Trainium2 kernel written in Bass

```python
import numpy as np
import jax
import jax.numpy as jnp

def _softmax(x, axis=-1):
    return jax.nn.softmax(x, axis=axis)

def _gelu(x):
    return jax.nn.gelu(x, approximate=True)

def _silu(x):
    return jax.nn.silu(x)

def _sigmoid(x):
    return jax.nn.sigmoid(x)

def _layernorm(x, axis=-1, eps=1e-05):
    m = jnp.mean(x, axis=axis, keepdims=True)
    v = jnp.var(x, axis=axis, keepdims=True)
    return (x - m) / jnp.sqrt(v + eps)

def _scatter_add(tgt, idx, src, axis=0):
    return tgt.at[idx].add(src)

def _segment_sum(src, seg, n):
    return jax.ops.segment_sum(src, seg, n)
kernel_name = 'mk_dlrm_tower_d1_rec_r8_4fa472'

def setup_inputs(seed: int=0):
    np.random.seed(seed)
    _w = jnp.asarray

    def _rec_inputs():
        import jax
        import jax.numpy as jnp
        _tk = jax.random.key(seed)
        ids = jnp.stack([jax.random.randint(jax.random.fold_in(_tk, 200 + f), (512,), 0, v, jnp.int32) for f, v in enumerate([125000, 12500, 1000, 1250, 12500, 12500, 1250, 12500, 1250, 1000, 1000, 1000, 1000, 1000, 1000, 1250, 1000, 12500, 1250, 1000, 12500, 1000, 1250, 1000, 12500, 1000])], axis=1)
        tbl_0 = 0.05 * jax.random.normal(jax.random.fold_in(_tk, 500 + 0), (125000, 128), jnp.float32)
        tbl_1 = 0.05 * jax.random.normal(jax.random.fold_in(_tk, 500 + 1), (12500, 128), jnp.float32)
        tbl_2 = 0.05 * jax.random.normal(jax.random.fold_in(_tk, 500 + 2), (1000, 128), jnp.float32)
        tbl_3 = 0.05 * jax.random.normal(jax.random.fold_in(_tk, 500 + 3), (1250, 128), jnp.float32)
        tbl_4 = 0.05 * jax.random.normal(jax.random.fold_in(_tk, 500 + 4), (12500, 128), jnp.float32)
        tbl_5 = 0.05 * jax.random.normal(jax.random.fold_in(_tk, 500 + 5), (12500, 128), jnp.float32)
        tbl_6 = 0.05 * jax.random.normal(jax.random.fold_in(_tk, 500 + 6), (1250, 128), jnp.float32)
        tbl_7 = 0.05 * jax.random.normal(jax.random.fold_in(_tk, 500 + 7), (12500, 128), jnp.float32)
        tbl_8 = 0.05 * jax.random.normal(jax.random.fold_in(_tk, 500 + 8), (1250, 128), jnp.float32)
        tbl_9 = 0.05 * jax.random.normal(jax.random.fold_in(_tk, 500 + 9), (1000, 128), jnp.float32)
        tbl_10 = 0.05 * jax.random.normal(jax.random.fold_in(_tk, 500 + 10), (1000, 128), jnp.float32)
        tbl_11 = 0.05 * jax.random.normal(jax.random.fold_in(_tk, 500 + 11), (1000, 128), jnp.float32)
        tbl_12 = 0.05 * jax.random.normal(jax.random.fold_in(_tk, 500 + 12), (1000, 128), jnp.float32)
        tbl_13 = 0.05 * jax.random.normal(jax.random.fold_in(_tk, 500 + 13), (1000, 128), jnp.float32)
        tbl_14 = 0.05 * jax.random.normal(jax.random.fold_in(_tk, 500 + 14), (1000, 128), jnp.float32)
        tbl_15 = 0.05 * jax.random.normal(jax.random.fold_in(_tk, 500 + 15), (1250, 128), jnp.float32)
        tbl_16 = 0.05 * jax.random.normal(jax.random.fold_in(_tk, 500 + 16), (1000, 128), jnp.float32)
        tbl_17 = 0.05 * jax.random.normal(jax.random.fold_in(_tk, 500 + 17), (12500, 128), jnp.float32)
        tbl_18 = 0.05 * jax.random.normal(jax.random.fold_in(_tk, 500 + 18), (1250, 128), jnp.float32)
        tbl_19 = 0.05 * jax.random.normal(jax.random.fold_in(_tk, 500 + 19), (1000, 128), jnp.float32)
        tbl_20 = 0.05 * jax.random.normal(jax.random.fold_in(_tk, 500 + 20), (12500, 128), jnp.float32)
        tbl_21 = 0.05 * jax.random.normal(jax.random.fold_in(_tk, 500 + 21), (1000, 128), jnp.float32)
        tbl_22 = 0.05 * jax.random.normal(jax.random.fold_in(_tk, 500 + 22), (1250, 128), jnp.float32)
        tbl_23 = 0.05 * jax.random.normal(jax.random.fold_in(_tk, 500 + 23), (1000, 128), jnp.float32)
        tbl_24 = 0.05 * jax.random.normal(jax.random.fold_in(_tk, 500 + 24), (12500, 128), jnp.float32)
        tbl_25 = 0.05 * jax.random.normal(jax.random.fold_in(_tk, 500 + 25), (1000, 128), jnp.float32)
        _rk = jax.random.fold_in(_tk, 7)
        r_dense = -0.000520686 + 1.00062 * jax.random.normal(jax.random.fold_in(_rk, 101), (512, 128), jnp.float32)
        W_top1 = 0.0456912 * jax.random.normal(jax.random.fold_in(_tk, 801), (479, 512), jnp.float32)
        W_top2 = 0.0441942 * jax.random.normal(jax.random.fold_in(_tk, 802), (512, 256), jnp.float32)
        W_top3 = 0.0625 * jax.random.normal(jax.random.fold_in(_tk, 803), (256, 1), jnp.float32)
        b_top1 = jnp.zeros((512,), jnp.float32)
        b_top2 = jnp.zeros((256,), jnp.float32)
        return (r_dense, ids, tbl_0, tbl_1, tbl_2, tbl_3, tbl_4, tbl_5, tbl_6, tbl_7, tbl_8, tbl_9, tbl_10, tbl_11, tbl_12, tbl_13, tbl_14, tbl_15, tbl_16, tbl_17, tbl_18, tbl_19, tbl_20, tbl_21, tbl_22, tbl_23, tbl_24, tbl_25, W_top1, b_top1, W_top2, b_top2, W_top3)
    r_dense, ids, tbl_0, tbl_1, tbl_2, tbl_3, tbl_4, tbl_5, tbl_6, tbl_7, tbl_8, tbl_9, tbl_10, tbl_11, tbl_12, tbl_13, tbl_14, tbl_15, tbl_16, tbl_17, tbl_18, tbl_19, tbl_20, tbl_21, tbl_22, tbl_23, tbl_24, tbl_25, W_top1, b_top1, W_top2, b_top2, W_top3 = _rec_inputs()

    def _L0_rec_setup():
        import jax, jax.numpy as jnp
        import numpy as np
        B, NUM_EMBS, D = (2048, 26, 128)
        key = jax.random.key(seed)
        k1, k2 = jax.random.split(key)
        dense = jax.random.normal(k1, (B, D), dtype=jnp.float32)
        embs = jax.random.normal(k2, (B, NUM_EMBS, D), dtype=jnp.float32)
        return {'dense': dense, 'embs': embs}
    _L0_rec_all = _L0_rec_setup()
    _L0_rec_in = {k: v for k, v in _L0_rec_all.items() if k in ()}
    del _L0_rec_all
    return {'r_dense': r_dense, 'ids': ids, 'tbl_0': tbl_0, 'tbl_1': tbl_1, 'tbl_2': tbl_2, 'tbl_3': tbl_3, 'tbl_4': tbl_4, 'tbl_5': tbl_5, 'tbl_6': tbl_6, 'tbl_7': tbl_7, 'tbl_8': tbl_8, 'tbl_9': tbl_9, 'tbl_10': tbl_10, 'tbl_11': tbl_11, 'tbl_12': tbl_12, 'tbl_13': tbl_13, 'tbl_14': tbl_14, 'tbl_15': tbl_15, 'tbl_16': tbl_16, 'tbl_17': tbl_17, 'tbl_18': tbl_18, 'tbl_19': tbl_19, 'tbl_20': tbl_20, 'tbl_21': tbl_21, 'tbl_22': tbl_22, 'tbl_23': tbl_23, 'tbl_24': tbl_24, 'tbl_25': tbl_25, 'W_top1': W_top1, 'b_top1': b_top1, 'W_top2': W_top2, 'b_top2': b_top2, 'W_top3': W_top3}

def reference(r_dense, ids, tbl_0, tbl_1, tbl_2, tbl_3, tbl_4, tbl_5, tbl_6, tbl_7, tbl_8, tbl_9, tbl_10, tbl_11, tbl_12, tbl_13, tbl_14, tbl_15, tbl_16, tbl_17, tbl_18, tbl_19, tbl_20, tbl_21, tbl_22, tbl_23, tbl_24, tbl_25, W_top1, b_top1, W_top2, b_top2, W_top3):
    import jax
    import jax.numpy as jnp

    def _L0_rec_ref(dense, embs):
        import jax, jax.numpy as jnp
        import numpy as np
        B, NUM_EMBS, D = (2048, 26, 128)
        T = jnp.concatenate([dense[:, None, :], embs], axis=1)
        N = T.shape[1]
        Z = jnp.einsum('bnd,bmd->bnm', T, T)
        iu0, iu1 = jnp.triu_indices(N, k=1)
        return Z[:, iu0, iu1]
    e = jnp.stack([tbl_0[ids[:, 0]], tbl_1[ids[:, 1]], tbl_2[ids[:, 2]], tbl_3[ids[:, 3]], tbl_4[ids[:, 4]], tbl_5[ids[:, 5]], tbl_6[ids[:, 6]], tbl_7[ids[:, 7]], tbl_8[ids[:, 8]], tbl_9[ids[:, 9]], tbl_10[ids[:, 10]], tbl_11[ids[:, 11]], tbl_12[ids[:, 12]], tbl_13[ids[:, 13]], tbl_14[ids[:, 14]], tbl_15[ids[:, 15]], tbl_16[ids[:, 16]], tbl_17[ids[:, 17]], tbl_18[ids[:, 18]], tbl_19[ids[:, 19]], tbl_20[ids[:, 20]], tbl_21[ids[:, 21]], tbl_22[ids[:, 22]], tbl_23[ids[:, 23]], tbl_24[ids[:, 24]], tbl_25[ids[:, 25]]], axis=1)
    z = _L0_rec_ref(r_dense, e)
    z = z.reshape(z.shape[0], -1)
    h = jnp.concatenate([z, r_dense], axis=1)
    h = jnp.maximum(h @ W_top1 + b_top1, 0.0)
    h = jnp.maximum(h @ W_top2 + b_top2, 0.0)
    y = h @ W_top3
    return y

_drawn_inputs = setup_inputs


def setup_inputs(seed=0):
    import zlib

    import numpy as np

    out = dict(_drawn_inputs(seed))
    spreads = {'b_top1': (0.0, 0.1), 'b_top2': (0.0, 0.1)}
    factors = {}
    for name, (base, spread) in spreads.items():
        noise = np.random.default_rng([zlib.crc32(name.encode()), seed]).standard_normal(out[name].shape)
        drawn = base * np.exp(spread * noise) if base else spread * noise
        out[name] = jnp.asarray(drawn.astype(out[name].dtype))
    for name, factor in factors.items():
        out[name] = (out[name] * factor).astype(out[name].dtype)
    return out
```

```python
import concourse.bass as bass
from concourse import mybir
from contextlib import ExitStack

P = 128
BATCH = 512
TILES = BATCH // P
TABLES = 26
ITEMS = TABLES + 1
SLOT = 32
QUADS = P // SLOT
GROUPS = P // QUADS
ITEM_GROUP = 4
ITEM_GROUPS = -(-ITEMS // ITEM_GROUP)
PARTNERS = ITEMS - 1
GROUPS_PER_BANK = 4
GRAM_BANKS = 2
GRAM_STEPS = GROUPS // (GROUPS_PER_BANK * GRAM_BANKS)
PAIR_COLS = 378
PAIR_CHUNKS = 3
PAIR_K = PAIR_COLS // PAIR_CHUNKS
H1, H2 = 512, 256
H1_CHUNKS, H2_CHUNKS = H1 // P, H2 // P
H1_HALF = H1_CHUNKS // 2


def pair_rectangles():
    return [
        (1, 28, 14, 0, 14, 14),
        (2, 14, 7, 0, 7, 7),
        (4, 7, 3, 0, 4, 3),
        (4, 7, 1, 0, 1, 1),
        (4, 7, 2, 0, 1, 2),
        (4, 7, 5, 3, 2, 2),
        (4, 7, 4, 3, 1, 1),
        (4, 7, 6, 5, 1, 1),
    ]


def pair_order():
    return [
        (g * apart + n0 + n, g * apart + m0 + m)
        for repeats, apart, m0, n0, ms, ns in pair_rectangles()
        for g in range(repeats)
        for m in range(ms)
        for n in range(ns)
    ]


def dlrm_tower(nc, ids, dense, tables, w1_pairs, w1_dense, w2, small, out):
    f32 = mybir.dt.float32
    u32 = mybir.dt.uint32
    ALU = mybir.AluOpType
    ACT = mybir.ActivationFunctionType

    with ExitStack() as ctx:
        def sb(name, shape, dt=f32):
            return ctx.enter_context(nc.sbuf_tensor(name, shape, dt))

        def ps(name, shape):
            return ctx.enter_context(nc.psum_tensor(name, shape, f32))

        def sem(name):
            return ctx.enter_context(nc.semaphore(name))

        index = sb("index", [P, TILES, TABLES], u32)
        rows = sb("rows", [P, TILES, ITEMS, P])
        ident = sb("ident", [P, P])
        items_t = sb("items_t", [P, TILES, GROUPS, QUADS, SLOT])
        dense_t = sb("dense_t", [P, P])
        pair_by_n = sb("pair_by_n", [P, 2, ITEMS, GROUPS])
        pair_by_b = sb("pair_by_b", [P, 36 * SLOT])
        pairs = sb("pairs", [P, PAIR_COLS])
        pairs_t = sb("pairs_t", [PAIR_K, PAIR_CHUNKS, P])
        h1_t = sb("h1_t", [P, H1_CHUNKS, P])
        h2_t = sb("h2_t", [P, H2_CHUNKS, P])
        y = sb("y", [P, TILES])
        w1p = sb("w1p", [PAIR_K, PAIR_CHUNKS, H1])
        w1d = sb("w1d", [P, H1])
        w2s = sb("w2s", [P, H1_CHUNKS, H2])
        smalls = sb("smalls", [P, H1_CHUNKS + 2 * H2_CHUNKS])
        b1 = smalls[:, 0:H1_CHUNKS]
        b2 = smalls[:, H1_CHUNKS:H1_CHUNKS + H2_CHUNKS]
        w3 = smalls[:, H1_CHUNKS + H2_CHUNKS:H1_CHUNKS + 2 * H2_CHUNKS]

        turned = [ps(f"turned{i}", [P, ITEM_GROUP, P]) for i in range(2)]
        gram = [ps(f"gram{i}", [P, GRAM_BANKS, 512]) for i in range(2)]
        mlp = [ps(f"mlp{i}", [P, 4, P]) for i in range(2)]

        ids_in = sem("ids_in")
        dense_in = sem("dense_in")
        w1_in = sem("w1_in")
        w2_in = sem("w2_in")
        small_in = sem("small_in")
        rows_in = [[sem(f"rows_in{t}_{q}") for q in range(ITEM_GROUPS)] for t in range(TILES)]
        ident_zero = sem("ident_zero")
        ident_done = sem("ident_done")
        pads_done = sem("pads_done")
        block_turned = sem("block_turned")
        block_moved = [sem("block_moved_dve"), sem("block_moved_act")]
        gram_done = sem("gram_done")
        gram_moved_dve = sem("gram_moved_dve")
        gram_moved_act = sem("gram_moved_act")
        pairs_by_sample = sem("pairs_by_sample")
        pairs_packed = sem("pairs_packed")
        h1_done = sem("h1_done")
        h1_moved = [sem("h1_moved_act"), sem("h1_moved_dve")]
        h2_done = sem("h2_done")
        h2_moved = [sem("h2_moved_act"), sem("h2_moved_dve")]
        y_done = sem("y_done")
        y_moved = sem("y_moved")
        out_done = sem("out_done")

        def group_items(q):
            return range(ITEM_GROUP * q, min(ITEM_GROUP * (q + 1), ITEMS))

        BLOCKS = ITEM_GROUPS + 1

        def block_bank(t, q):
            return (BLOCKS * t + q) % 2, (BLOCKS * t + q) // 2

        block = ctx.enter_context(nc.Block())

        @block.sync
        def _(sp):
            sp.dma_start(index[:, :, :], ids.rearrange("(p t) f -> p t f", t=TILES).bitcast(u32)).then_inc(ids_in, 16)
            sp.dma_start(rows[:, :, 0, :], dense.rearrange("(p t) d -> p t d", t=TILES)).then_inc(dense_in, 16)
            sp.dma_start(w1p[:, :, :], w1_pairs.rearrange("(c k) n -> k c n", k=PAIR_K)).then_inc(w1_in, 16)
            sp.dma_start(w1d[:, :], w1_dense).then_inc(w1_in, 16)
            sp.dma_start(w2s[:, :, :], w2.rearrange("(c k) n -> k c n", k=P)).then_inc(w2_in, 16)
            sp.dma_start(smalls[:, :], small).then_inc(small_in, 16)
            sp.wait_ge(y_moved, TILES)
            sp.dma_start(out.rearrange("(p t) o -> p (t o)", t=TILES), y[:, :]).then_inc(out_done, 16)
            sp.wait_ge(out_done, 16)

        @block.gpsimd
        def _(pool):
            nc.gpsimd.memset(ident[:, :], 0.0).then_inc(ident_zero, 1)
            pool.wait_ge(ident_zero, 1)
            nc.gpsimd.affine_select(out=ident[:, :], in_=ident[:, :], compare_op=ALU.not_equal, fill=1.0, base=0,
                                    pattern=[[-1, P]], channel_multiplier=1).then_inc(ident_done, 1)
            pool.wait_ge(ids_in, 16)
            for t in range(TILES):
                for q in range(ITEM_GROUPS):
                    for i in group_items(q):
                        if i == 0:
                            continue
                        pool.indirect_dma_start(
                            rows[:, t, i, :], None, tables[i - 1][:, :],
                            bass.IndirectOffsetOnAxis(ap=index[:, t, i - 1:i], axis=0),
                        ).then_inc(rows_in[t][q], 16)

        @block.tensor
        def _(pe):
            pe.wait_ge(ident_done, 1)
            pe.wait_ge(dense_in, 16)
            for t in range(TILES):
                for q in range(ITEM_GROUPS):
                    gathered = len([i for i in group_items(q) if i > 0])
                    bank, before = block_bank(t, q)
                    pe.wait_ge(rows_in[t][q], 16 * gathered)
                    if before:
                        pe.wait_ge(block_moved[bank], before)
                    for k, i in enumerate(group_items(q)):
                        last = nc.tensor.transpose(turned[bank][:, k, :], rows[:, t, i, :], ident[:, :])
                    last.then_inc(block_turned, 1)
                for parity in range(2):
                    bank, before = block_bank(t, ITEM_GROUPS - 1 - parity)
                    pe.wait_ge(block_moved[bank], before + 1)
                pe.wait_ge(pads_done, 1)
                for s in range(GRAM_STEPS):
                    step = GRAM_STEPS * t + s
                    if step >= 2:
                        pe.wait_ge(gram_moved_dve, step - 1)
                        pe.wait_ge(gram_moved_act, step - 1)
                    for bank in range(GRAM_BANKS):
                        for k in range(GROUPS_PER_BANK):
                            group = (s * GRAM_BANKS + bank) * GROUPS_PER_BANK + k
                            samples = items_t[:, t, group, :, :]
                            cols = QUADS * PARTNERS
                            last = nc.tensor.matmul(gram[step % 2][:, bank, cols * k:cols * (k + 1)],
                                                    samples.rearrange("d j i -> d (j i)"), samples[:, :, 1:ITEMS], start=True, stop=True)
                    last.then_inc(gram_done, 1)
                bank, before = block_bank(t, ITEM_GROUPS)
                pe.wait_ge(block_moved[bank], before)
                pe.wait_ge(pairs_packed, t + 1)
                for c in range(PAIR_CHUNKS):
                    last = nc.tensor.transpose(turned[bank][0:PAIR_K, c, :], pairs[:, PAIR_K * c:PAIR_K * (c + 1)], ident[:, :])
                last.then_inc(block_turned, 1)
                if t == 0:
                    pe.wait_ge(w1_in, 32)
                for j in range(H1_CHUNKS):
                    cols = slice(P * j, P * (j + 1))
                    side, k = j // H1_HALF, j % H1_HALF
                    if t > 0 and k == 0:
                        pe.wait_ge(*[(h2_moved[0], t), (y_moved, t)][side])
                    nc.tensor.matmul(mlp[side][:, k, :], w1d[:, cols], dense_t[:, :], start=True, stop=False)
                    if j == 0:
                        pe.wait_ge(block_moved[bank], before + 1)
                    for c in range(PAIR_CHUNKS):
                        last = nc.tensor.matmul(mlp[side][:, k, :], w1p[:, c, cols], pairs_t[:, c, :],
                                                start=False, stop=(c == PAIR_CHUNKS - 1))
                    if k == H1_HALF - 1:
                        last.then_inc(h1_done, 1)
                if t == 0:
                    pe.wait_ge(w2_in, 16)
                pe.wait_ge(h1_moved[0], H1_HALF * (t + 1))
                for j in range(H2_CHUNKS):
                    for c in range(H1_CHUNKS):
                        if j == 0 and c >= H1_HALF:
                            pe.wait_ge(h1_moved[1], H1_HALF * t + c - H1_HALF + 1)
                        last = nc.tensor.matmul(mlp[j][:, 0, :], w2s[:, c, P * j:P * (j + 1)], h1_t[:, c, :],
                                                start=(c == 0), stop=(c == H1_CHUNKS - 1))
                    last.then_inc(h2_done, 1)
                pe.wait_ge(small_in, 16)
                pe.wait_ge(h2_moved[0], t + 1)
                pe.wait_ge(h2_moved[1], t + 1)
                for c in range(H2_CHUNKS):
                    last = nc.tensor.matmul(mlp[1][:, 1, 0:1], h2_t[:, c, :], w3[:, c:c + 1],
                                            start=(c == 0), stop=(c == H2_CHUNKS - 1))
                last.then_inc(y_done, 1)

        def item_view(t, q):
            lo, hi = group_items(q)[0], group_items(q)[-1] + 1
            return items_t[:, t, :, :, lo:hi].rearrange("d g j i -> d i j g")

        def turned_view(t, q):
            bank, _ = block_bank(t, q)
            return turned[bank][:, 0:len(group_items(q)), :].rearrange("d i (j g) -> d i j g", j=QUADS)

        def gram_views(t, s, j):
            cols = QUADS * PARTNERS
            part = slice(SLOT * j, SLOT * (j + 1))
            src = gram[(GRAM_STEPS * t + s) % 2][part, :, 0:GROUPS_PER_BANK * cols]
            src = src.rearrange("n b (k j m) -> n b k j m", j=QUADS, m=PARTNERS)[:, :, :, j, :]
            per_step = GRAM_BANKS * GROUPS_PER_BANK
            dst = pair_by_n[part, t % 2, 0:PARTNERS, per_step * s:per_step * (s + 1)]
            dst = dst.rearrange("n m (b k) -> n b k m", k=GROUPS_PER_BANK)
            return dst, src

        @block.vector
        def _(dve):
            nc.vector.memset(items_t[:, :, :, :, ITEMS:SLOT].rearrange("d t g j i -> d (t g j) i"), 0.0).then_inc(pads_done, 1)
            nc.vector.memset(pair_by_n[:, :, PARTNERS, :], 0.0)
            for t in range(TILES):
                for q in range(ITEM_GROUPS):
                    if block_bank(t, q)[0]:
                        continue
                    dve.wait_ge(block_turned, BLOCKS * t + q + 1)
                    if q == 0:
                        nc.vector.tensor_copy(dense_t[:, :], turned[0][:, 0, :])
                    nc.vector.tensor_copy(item_view(t, q), turned_view(t, q)).then_inc(block_moved[0], 1)
                for s in range(GRAM_STEPS):
                    dve.wait_ge(gram_done, GRAM_STEPS * t + s + 1)
                    for j in range(0, 2):
                        last = nc.vector.tensor_copy(*gram_views(t, s, j))
                    last.then_inc(gram_moved_dve, 1)
                dve.wait_ge(gram_moved_dve, GRAM_STEPS * (t + 1))
                dve.wait_ge(gram_moved_act, GRAM_STEPS * (t + 1))
                nc.vector.transpose(pair_by_b[:, 0:ITEMS * SLOT],
                                    pair_by_n[:, t % 2, :, :].rearrange("n m g -> n (m g)")).then_inc(pairs_by_sample, 1)
                dve.wait_ge(pairs_by_sample, t + 1)
                at = 0
                for repeats, apart, m0, n0, ms, ns in pair_rectangles():
                    first, stride = SLOT * (m0 - 1) + n0, apart * (SLOT + 1)
                    src = pair_by_b[:, first:first + repeats * stride] if repeats > 1 else pair_by_b[:, first:first + SLOT * ms]
                    src = src.rearrange("b (g x) -> b g x", g=repeats)[:, :, 0:min(SLOT * ms, src.shape[1] // repeats)]
                    src = src.rearrange("b g (m n) -> b g m n", m=ms)[:, :, :, 0:ns]
                    size = repeats * ms * ns
                    dst = pairs[:, at:at + size].rearrange("b (g m n) -> b g m n", g=repeats, m=ms)
                    last = nc.vector.tensor_copy(dst, src)
                    at += size
                last.then_inc(pairs_packed, 1)
                if t == 0:
                    dve.wait_ge(small_in, 16)
                dve.wait_ge(h1_done, 2 * t + 2)
                for j in range(H1_HALF, H1_CHUNKS):
                    nc.vector.tensor_scalar(h1_t[:, j, :], mlp[1][:, j - H1_HALF, :], b1[:, j:j + 1], 0.0, ALU.add, ALU.max).then_inc(h1_moved[1], 1)
                dve.wait_ge(h2_done, H2_CHUNKS * t + 2)
                nc.vector.tensor_scalar(h2_t[:, 1, :], mlp[1][:, 0, :], b2[:, 1:2], 0.0, ALU.add, ALU.max).then_inc(h2_moved[1], 1)
                dve.wait_ge(y_done, t + 1)
                nc.vector.tensor_copy(y[:, t:t + 1], mlp[1][:, 1, 0:1]).then_inc(y_moved, 1)

        @block.scalar
        def _(act):
            for t in range(TILES):
                for q in range(ITEM_GROUPS):
                    if not block_bank(t, q)[0]:
                        continue
                    act.wait_ge(block_turned, BLOCKS * t + q + 1)
                    nc.scalar.copy(item_view(t, q), turned_view(t, q)).then_inc(block_moved[1], 1)
                if t >= 2:
                    act.wait_ge(pairs_by_sample, t - 1)
                for s in range(GRAM_STEPS):
                    act.wait_ge(gram_done, GRAM_STEPS * t + s + 1)
                    for j in range(2, QUADS):
                        last = nc.scalar.copy(*gram_views(t, s, j))
                    last.then_inc(gram_moved_act, 1)
                act.wait_ge(block_turned, BLOCKS * (t + 1))
                nc.scalar.copy(pairs_t[:, :, :], turned[1][0:PAIR_K, 0:PAIR_CHUNKS, :]).then_inc(block_moved[1], 1)
                if t == 0:
                    act.wait_ge(small_in, 16)
                act.wait_ge(h1_done, 2 * t + 1)
                for j in range(H1_HALF):
                    nc.scalar.activation(h1_t[:, j, :], mlp[0][:, j, :], ACT.Relu, bias=b1[:, j:j + 1]).then_inc(h1_moved[0], 1)
                act.wait_ge(h2_done, H2_CHUNKS * t + 1)
                nc.scalar.activation(h2_t[:, 0, :], mlp[0][:, 0, :], ACT.Relu, bias=b2[:, 0:1]).then_inc(h2_moved[0], 1)


def kernel(**inputs):
    import numpy as np
    import concourse.bacc as bacc
    from concourse import mybir
    from concourse.bass_utils import run_bass_kernel_spmd as run

    nc = bacc.Bacc("TRN2", target_bir_lowering=False, num_devices=1)
    arrays = {}

    def put(name, a):
        arrays[name] = a = np.ascontiguousarray(a)
        return nc.dram_tensor(name, a.shape, mybir.dt.from_np(a.dtype), kind="ExternalInput").ap()

    w1 = np.asarray(inputs["W_top1"])
    order = pair_order()
    w1_pairs = np.zeros((PAIR_COLS, H1), w1.dtype)
    for row, (n, m) in enumerate(order):
        if m < ITEMS:
            w1_pairs[row] = w1[n * ITEMS - n * (n + 1) // 2 + m - n - 1]
    n_pairs = ITEMS * (ITEMS - 1) // 2
    small = np.concatenate([
        np.asarray(inputs["b_top1"]).reshape(H1_CHUNKS, P).T,
        np.asarray(inputs["b_top2"]).reshape(H2_CHUNKS, P).T,
        np.asarray(inputs["W_top3"]).reshape(H2_CHUNKS, P).T,
    ], axis=1)
    args = [put("ids", inputs["ids"]), put("dense", inputs["r_dense"])]
    tables = [put(f"tbl_{f}", inputs[f"tbl_{f}"]) for f in range(TABLES)]
    args += [tables, put("w1_pairs", w1_pairs), put("w1_dense", w1[n_pairs:]), put("w2", inputs["W_top2"]), put("small", small)]
    out = nc.dram_tensor("y_out", (BATCH, 1), mybir.dt.float32, kind="ExternalOutput").ap()
    dlrm_tower(nc, *args, out)
    r = run(nc, [arrays], core_ids=[0])
    return r.results[0]["y_out"]
```

```python
import concourse.bass as bass
from concourse import mybir
from contextlib import ExitStack

P = 128
BATCH = 512
TILES = BATCH // P
TABLES = 26

LOOKED_UP = [2, 9, 10, 11, 12, 13, 14, 16, 19]
LOOKUP_ROWS = 1000
LOOKUP_CHUNKS = 8
LOOKUP_K = LOOKUP_ROWS // LOOKUP_CHUNKS
LOOKUP_SPRAY = 112
GATHERED = [f for f in range(TABLES) if f not in LOOKED_UP]
LOOKUPS = len(LOOKED_UP)

ITEM_TABLE = [None] + GATHERED + LOOKED_UP
ITEMS = len(ITEM_TABLE)
TURNED_ITEMS = 1 + len(GATHERED)
SLOT = 32
QUADS = P // SLOT
GROUPS = P // QUADS
ITEM_GROUP = 4
ITEM_GROUPS = -(-TURNED_ITEMS // ITEM_GROUP)
PARTNERS = ITEMS - 1
STATIONARY = (QUADS - 1) * SLOT + ITEMS - 1
GROUPS_PER_BANK = 4
GRAM_BANKS = 2
GRAM_STEPS = GROUPS // (GROUPS_PER_BANK * GRAM_BANKS)
PAIR_COLS = 378
PAIR_CHUNKS = 3
PAIR_K = PAIR_COLS // PAIR_CHUNKS
H1, H2 = 512, 256
H1_CHUNKS, H2_CHUNKS = H1 // P, H2 // P
H1_HALF = H1_CHUNKS // 2
TABLE_BUFS = 3
SPLIT_BUFS = 2
LOOKUP_HALVES = 2
HALF_CHUNKS = LOOKUP_CHUNKS // LOOKUP_HALVES
WARM_UP = 14

LOOKUP = "lookup"
TURN = "turn"
GRAM = "gram"
PACK = "pack"
PAIRS = "pairs"
LAYER1, LAYER2, SCORE = "layer1", "layer2", "score"


def step_order():
    early = [(TURN, (t, q)) for t in range(2) for q in range(ITEM_GROUPS)]
    order = []
    for k in range(LOOKUPS):
        order.append((LOOKUP, k))
        if k and early:
            order.append(early.pop(0))
    order += early
    order += [(GRAM, (0, s)) for s in range(GRAM_STEPS)] + [(PACK, 0)]
    for t in range(1, TILES):
        turns = [(TURN, (t + 1, q)) for q in range(ITEM_GROUPS)] if t + 1 < TILES else []
        score = [(SCORE, t - 2)] if t >= 2 else []
        if t < TILES - 1:
            layers = [score, [(PAIRS, t - 1)], [(LAYER1, t - 1)], [(LAYER2, t - 1), (PACK, t)]]
        else:
            layers = [score, [(PAIRS, t - 1)], [], [(PACK, t), (LAYER1, t - 1), (PAIRS, t), (LAYER2, t - 1), (SCORE, t - 1)]]
        for s in range(GRAM_STEPS):
            at = [ITEM_GROUPS * i // GRAM_STEPS for i in (s, s + 1)]
            order += [(GRAM, (t, s))] + turns[at[0]:at[1]] + layers[s]
    return order + [(kind, TILES - 1) for kind in (LAYER1, LAYER2, SCORE)]


ORDER = step_order()


def block_owners():
    owners, counts = {}, {"act": 0, "dve": 0}
    first_gram = ORDER.index((GRAM, (0, 0)))
    for at, step in enumerate(ORDER):
        if step[0] not in (LOOKUP, TURN, PAIRS):
            continue
        late = step[0] == TURN and step[1][0] >= 2
        engine = "dve" if late and step[1][1] % 2 == 0 else "act"
        counts[engine] += 1
        bank = len(owners) % (BLOCK_BANKS if at < first_gram else 2)
        owners[step] = (len(owners), bank, engine, counts[engine])
    return owners


BLOCK_BANKS = 4
BLOCKS = block_owners()


def bank_before(step):
    number, bank, _, _ = BLOCKS[step]
    before = [s for s in BLOCKS if BLOCKS[s][0] < number and BLOCKS[s][1] == bank]
    return before[-1] if before else None


def pair_rectangles():
    return [
        (1, 28, 14, 0, 14, 14),
        (2, 14, 7, 0, 7, 7),
        (4, 7, 3, 0, 4, 3),
        (4, 7, 1, 0, 1, 1),
        (4, 7, 2, 0, 1, 2),
        (4, 7, 5, 3, 2, 2),
        (4, 7, 4, 3, 1, 1),
        (4, 7, 6, 5, 1, 1),
    ]


def pair_order():
    return [
        (g * apart + n0 + n, g * apart + m0 + m)
        for repeats, apart, m0, n0, ms, ns in pair_rectangles()
        for g in range(repeats)
        for m in range(ms)
        for n in range(ns)
    ]


def dlrm_tower(nc, ids, ids_by_table, dense, tables, w1_pairs, w1_dense, w2, small, out):
    f32 = mybir.dt.float32
    f32r = mybir.dt.float32r
    i32 = mybir.dt.int32
    u32 = mybir.dt.uint32
    ALU = mybir.AluOpType
    ACT = mybir.ActivationFunctionType

    with ExitStack() as ctx:
        def sb(name, shape, dt=f32):
            return ctx.enter_context(nc.sbuf_tensor(name, shape, dt))

        def ps(name, shape):
            return ctx.enter_context(nc.psum_tensor(name, shape, f32))

        def sem(name):
            return ctx.enter_context(nc.semaphore(name))

        index = sb("index", [P, TILES, TABLES], u32)
        rows = sb("rows", [P, TILES, TURNED_ITEMS, P])
        wanted = sb("wanted", [P, TABLE_BUFS, BATCH], i32)
        table = sb("table", [P, TABLE_BUFS, LOOKUP_CHUNKS, P])
        table_hi = sb("table_hi", [P, SPLIT_BUFS, LOOKUP_CHUNKS, P], f32r)
        table_lo = sb("table_lo", [P, SPLIT_BUFS, LOOKUP_CHUNKS, P], f32r)
        one_hot = sb("one_hot", [P, 2, LOOKUP_CHUNKS, BATCH], f32r)
        first_row = sb("first_row", [P, 1])
        minus_first_row = sb("minus_first_row", [P, 1])
        wanted_chunk = sb("wanted_chunk", [P, 2, BATCH])
        ident = sb("ident", [P, P])
        zeros = sb("zeros", [P, P])
        items_t = sb("items_t", [P, TILES, GROUPS, QUADS, SLOT])
        dense_t = sb("dense_t", [P, TILES, P])
        pair_by_n = sb("pair_by_n", [P, 2, ITEMS, GROUPS])
        pair_by_b = sb("pair_by_b", [P, 36 * SLOT])
        pairs = sb("pairs", [P, 2, PAIR_COLS])
        pairs_t = sb("pairs_t", [PAIR_K, PAIR_CHUNKS, P])
        h1_t = sb("h1_t", [P, H1_CHUNKS, P])
        h2_t = sb("h2_t", [P, H2_CHUNKS, P])
        y = sb("y", [P, TILES])
        w1p = sb("w1p", [PAIR_K, PAIR_CHUNKS, H1])
        w1d = sb("w1d", [P, H1])
        w2s = sb("w2s", [P, H1_CHUNKS, H2])
        smalls = sb("smalls", [P, H1_CHUNKS + 2 * H2_CHUNKS])
        b1 = smalls[:, 0:H1_CHUNKS]
        b2 = smalls[:, H1_CHUNKS:H1_CHUNKS + H2_CHUNKS]
        w3 = smalls[:, H1_CHUNKS + H2_CHUNKS:H1_CHUNKS + 2 * H2_CHUNKS]

        blocks = [ps(f"block{i}", [P, ITEM_GROUP, P]) for i in range(BLOCK_BANKS)]
        gram = [ps(f"gram{i}", [P, GRAM_BANKS, 512]) for i in range(2)]
        mlp = blocks[2:4]

        ids_in = sem("ids_in")
        dense_in = sem("dense_in")
        wanted_in = [sem(f"wanted_in{k}") for k in range(LOOKUPS)]
        table_in = [[sem(f"table_in{k}_{h}") for h in range(LOOKUP_HALVES)] for k in range(LOOKUPS)]
        numbered = sem("numbered")
        negated = sem("negated")
        hi_done = sem("hi_done")
        lo_done = sem("lo_done")
        chunk_done = sem("chunk_done")
        one_hot_done = sem("one_hot_done")
        w1_in = sem("w1_in")
        w2_in = sem("w2_in")
        small_in = sem("small_in")
        rows_in = [[sem(f"rows_in{t}_{q}") for q in range(ITEM_GROUPS)] for t in range(TILES)]
        ident_zero = sem("ident_zero")
        ident_done = sem("ident_done")
        pads_done = sem("pads_done")
        pairs_cleared = sem("pairs_cleared")
        block_done = sem("block_done")
        block_moved = {"act": sem("block_moved_act"), "dve": sem("block_moved_dve")}
        gram_done = sem("gram_done")
        gram_moved_dve = sem("gram_moved_dve")
        gram_moved_act = sem("gram_moved_act")
        pairs_by_sample = sem("pairs_by_sample")
        pairs_packed = sem("pairs_packed")
        h1_done = sem("h1_done")
        h1_moved = [sem("h1_moved_act"), sem("h1_moved_dve")]
        h2_done = sem("h2_done")
        h2_moved = [sem("h2_moved_act"), sem("h2_moved_dve")]
        y_done = sem("y_done")
        y_moved = sem("y_moved")
        out_done = sem("out_done")

        def group_items(q):
            return range(ITEM_GROUP * q, min(ITEM_GROUP * (q + 1), TURNED_ITEMS))

        block = ctx.enter_context(nc.Block())

        @block.sync
        def _(sp):
            for k, f in enumerate(LOOKED_UP):
                if k >= TABLE_BUFS:
                    sp.wait_ge(chunk_done, k - TABLE_BUFS + 1)
                    sp.wait_ge(hi_done, LOOKUP_HALVES * (k - TABLE_BUFS + 1))
                    sp.wait_ge(lo_done, LOOKUP_HALVES * (k - TABLE_BUFS + 1))
                src = tables[f].rearrange("(k c) d -> k c d", c=LOOKUP_CHUNKS)
                for h in range(LOOKUP_HALVES):
                    half = slice(HALF_CHUNKS * h, HALF_CHUNKS * (h + 1))
                    for part in (slice(0, LOOKUP_SPRAY), slice(LOOKUP_SPRAY, LOOKUP_K)):
                        sp.dma_start(table[part, k % TABLE_BUFS, half, :], src[part, half, :]).then_inc(table_in[k][h], 16)
                if k >= 1:
                    sp.dma_start(wanted[:, k % TABLE_BUFS, :], ids_by_table[f:f + 1, :].to_broadcast([P, BATCH])).then_inc(wanted_in[k], 16)
                if k == 0:
                    sp.dma_start(rows[:, :, 0, :], dense.rearrange("(p t) d -> p t d", t=TILES)).then_inc(dense_in, 16)
            sp.dma_start(w1p[:, :, :], w1_pairs.rearrange("(c k) n -> k c n", k=PAIR_K)).then_inc(w1_in, 16)
            sp.dma_start(w1d[:, :], w1_dense).then_inc(w1_in, 16)
            sp.dma_start(w2s[:, :, :], w2.rearrange("(c k) n -> k c n", k=P)).then_inc(w2_in, 16)
            sp.dma_start(smalls[:, :], small).then_inc(small_in, 16)
            sp.wait_ge(y_moved, TILES)
            sp.dma_start(out.rearrange("(p t) o -> p (t o)", t=TILES), y[:, :]).then_inc(out_done, 16)
            sp.wait_ge(out_done, 16)

        @block.gpsimd
        def _(pool):
            nc.gpsimd.iota(first_row[:, :], pattern=[[0, 1]], base=0, channel_multiplier=LOOKUP_CHUNKS,
                           allow_small_or_imprecise_dtypes=True).then_inc(numbered, 1)
            nc.gpsimd.memset(zeros[:, :], 0.0)
            nc.gpsimd.memset(ident[:, :], 0.0).then_inc(ident_zero, 1)
            pool.wait_ge(ident_zero, 1)
            nc.gpsimd.affine_select(out=ident[:, :], in_=ident[:, :], compare_op=ALU.not_equal, fill=1.0, base=0,
                                    pattern=[[-1, P]], channel_multiplier=1).then_inc(ident_done, 1)
            pool.wait_ge(ids_in, 16)
            for t in range(TILES):
                for q in range(ITEM_GROUPS):
                    for i in group_items(q):
                        if i == 0:
                            continue
                        pool.indirect_dma_start(
                            rows[:, t, i, :], None, tables[ITEM_TABLE[i]][:, :],
                            bass.IndirectOffsetOnAxis(ap=index[:, t, ITEM_TABLE[i]:ITEM_TABLE[i] + 1], axis=0),
                        ).then_inc(rows_in[t][q], 16)

        @block.tensor
        def _(pe):
            def bank_free(step):
                before = bank_before(step)
                if before:
                    _, _, engine, count = BLOCKS[before]
                    pe.wait_ge(block_moved[engine], count)
                return blocks[BLOCKS[step][1]]

            def lookup(k):
                out_d = bank_free((LOOKUP, k))[:, :, :].rearrange("d i b -> d (i b)")
                for h in range(LOOKUP_HALVES):
                    for part, part_done in ((table_hi, hi_done), (table_lo, lo_done)):
                        pe.wait_ge(part_done, LOOKUP_HALVES * k + h + 1)
                        for c in range(HALF_CHUNKS * h, HALF_CHUNKS * (h + 1)):
                            if part is table_hi:
                                pe.wait_ge(one_hot_done, LOOKUP_CHUNKS * k + c + 1)
                            last = nc.tensor.matmul(out_d, part[0:LOOKUP_K, k % SPLIT_BUFS, c, :], one_hot[0:LOOKUP_K, k % 2, c, :],
                                                    start=(part is table_hi and c == 0),
                                                    stop=(part is table_lo and c == LOOKUP_CHUNKS - 1))
                last.then_inc(block_done, 1)

            def turn(t, q):
                gathered = len([i for i in group_items(q) if i > 0])
                bank = bank_free((TURN, (t, q)))
                pe.wait_ge(rows_in[t][q], 16 * gathered)
                if t == 0 and q == 0:
                    pe.wait_ge(ident_done, 1)
                    pe.wait_ge(dense_in, 16)
                for k, i in enumerate(group_items(q)):
                    last = nc.tensor.transpose(bank[:, k, :], rows[:, t, i, :], ident[:, :])
                last.then_inc(block_done, 1)

            def products(t, s):
                if s == 0:
                    needed = [(TURN, (t, q)) for q in range(ITEM_GROUPS)] + [(LOOKUP, k) for k in range(LOOKUPS)]
                    for name in ("act", "dve"):
                        counts = [BLOCKS[x][3] for x in needed if BLOCKS[x][2] == name]
                        if counts:
                            pe.wait_ge(block_moved[name], max(counts))
                    if t == 0:
                        pe.wait_ge(pads_done, 1)
                step = GRAM_STEPS * t + s
                if step >= 2:
                    pe.wait_ge(gram_moved_dve, step - 1)
                    pe.wait_ge(gram_moved_act, step - 1)
                cols = QUADS * PARTNERS
                for bank in range(GRAM_BANKS):
                    for k in range(GROUPS_PER_BANK):
                        samples = items_t[:, t, (s * GRAM_BANKS + bank) * GROUPS_PER_BANK + k, :, :]
                        last = nc.tensor.matmul(gram[step % 2][0:STATIONARY, bank, cols * k:cols * (k + 1)],
                                                samples.rearrange("d j i -> d (j i)")[:, 0:STATIONARY], samples[:, :, 1:ITEMS],
                                                start=True, stop=True)
                last.then_inc(gram_done, 1)

            def turn_pairs(t):
                bank = bank_free((PAIRS, t))
                pe.wait_ge(pairs_packed, t + 1)
                for c in range(PAIR_CHUNKS):
                    last = nc.tensor.transpose(bank[0:PAIR_K, c, :], pairs[:, t % 2, PAIR_K * c:PAIR_K * (c + 1)], ident[:, :])
                last.then_inc(block_done, 1)

            def layer1(t):
                if t == 0:
                    pe.wait_ge(w1_in, 32)
                for side in range(2):
                    if t > 0:
                        pe.wait_ge(*[(h2_moved[0], t), (y_moved, t)][side])
                    for k in range(H1_HALF):
                        j = side * H1_HALF + k
                        nc.tensor.matmul(mlp[side][:, k, :], w1d[:, P * j:P * (j + 1)], dense_t[:, t, :], start=(k == 0), stop=False)
                _, _, engine, count = BLOCKS[(PAIRS, t)]
                pe.wait_ge(block_moved[engine], count)
                for side in range(2):
                    for k in range(H1_HALF):
                        j = side * H1_HALF + k
                        for c in range(PAIR_CHUNKS):
                            last = nc.tensor.matmul(mlp[side][:, k, :], w1p[:, c, P * j:P * (j + 1)], pairs_t[:, c, :], start=False,
                                                    stop=(k == H1_HALF - 1 and c == PAIR_CHUNKS - 1))
                    last.then_inc(h1_done, 1)

            def layer2(t):
                if t == 0:
                    pe.wait_ge(w2_in, 16)
                pe.wait_ge(h1_moved[0], H1_HALF * (t + 1))
                for j in range(H2_CHUNKS):
                    for c in range(H1_CHUNKS):
                        if j == 0 and c >= H1_HALF:
                            pe.wait_ge(h1_moved[1], H1_HALF * t + c - H1_HALF + 1)
                        last = nc.tensor.matmul(mlp[j][:, 0, :], w2s[:, c, P * j:P * (j + 1)], h1_t[:, c, :],
                                                start=(c == 0), stop=(c == H1_CHUNKS - 1))
                    last.then_inc(h2_done, 1)

            def score(t):
                if t == 0:
                    pe.wait_ge(small_in, 16)
                for c in range(H2_CHUNKS):
                    pe.wait_ge(h2_moved[1 - c], t + 1)
                    last = nc.tensor.matmul(mlp[1][:, 1, 0:1], h2_t[:, 1 - c, :], w3[:, 1 - c:2 - c],
                                            start=(c == 0), stop=(c == H2_CHUNKS - 1))
                last.then_inc(y_done, 1)

            pe.wait_ge(ident_zero, 1)
            for _ in range(WARM_UP):
                nc.tensor.matmul(gram[0][:, 0, 0:P], zeros[:, :], zeros[:, :], start=True, stop=True)
            do = {LOOKUP: lookup, PAIRS: turn_pairs, LAYER1: layer1, LAYER2: layer2, SCORE: score}
            for kind, which in ORDER:
                if kind == TURN:
                    turn(*which)
                elif kind == GRAM:
                    products(*which)
                elif kind in do:
                    do[kind](which)

        def looked_up_views(k):
            src = blocks[BLOCKS[(LOOKUP, k)][1]][:, :, :].rearrange("d i b -> d (i b)").rearrange("d (j g t) -> d j g t", j=QUADS, t=TILES)
            return items_t[:, :, :, :, TURNED_ITEMS + k].rearrange("d t g j -> d j g t"), src

        def turned_views(t, q):
            lo, hi = group_items(q)[0], group_items(q)[-1] + 1
            src = blocks[BLOCKS[(TURN, (t, q))][1]][:, 0:hi - lo, :].rearrange("d i (j g) -> d i j g", j=QUADS)
            return items_t[:, t, :, :, lo:hi].rearrange("d g j i -> d i j g"), src

        def gram_views(t, s, j):
            cols = QUADS * PARTNERS
            part = slice(SLOT * j, min(SLOT * (j + 1), STATIONARY))
            src = gram[(GRAM_STEPS * t + s) % 2][part, :, 0:GROUPS_PER_BANK * cols]
            src = src.rearrange("n b (k j m) -> n b k j m", j=QUADS, m=PARTNERS)[:, :, :, j, :]
            per_step = GRAM_BANKS * GROUPS_PER_BANK
            dst = pair_by_n[part, t % 2, 0:PARTNERS, per_step * s:per_step * (s + 1)]
            dst = dst.rearrange("n m (b k) -> n b k m", k=GROUPS_PER_BANK)
            return dst, src

        @block.vector
        def _(dve):
            def one_hot_of(k):
                if k >= 2:
                    dve.wait_ge(block_done, BLOCKS[(LOOKUP, k - 2)][0] + 1)
                for c in range(LOOKUP_CHUNKS):
                    if c % HALF_CHUNKS == 1:
                        half = slice(c - 1, c - 1 + HALF_CHUNKS)
                        dve.wait_ge(table_in[k][c // HALF_CHUNKS], 32)
                        dve.wait_ge(hi_done, LOOKUP_HALVES * k + c // HALF_CHUNKS + 1)
                        nc.vector.tensor_tensor(table_lo[0:LOOKUP_K, k % SPLIT_BUFS, half, :], table[0:LOOKUP_K, k % TABLE_BUFS, half, :],
                                                table_hi[0:LOOKUP_K, k % SPLIT_BUFS, half, :].bitcast(f32), ALU.subtract).then_inc(lo_done, 1)
                    if c == 0:
                        dve.wait_ge(chunk_done, k + 1)
                    nc.vector.tensor_scalar(one_hot[0:LOOKUP_K, k % 2, c, :], wanted_chunk[0:LOOKUP_K, k % 2, :],
                                            float(c), None, ALU.is_equal).then_inc(one_hot_done, 1)

            def turned_block(t, q):
                if BLOCKS[(TURN, (t, q))][2] != "dve":
                    return
                dve.wait_ge(block_done, BLOCKS[(TURN, (t, q))][0] + 1)
                dst, src = turned_views(t, q)
                if q == 0:
                    nc.vector.tensor_copy(dense_t[:, t, :], blocks[BLOCKS[(TURN, (t, q))][1]][:, 0, :])
                nc.vector.tensor_copy(dst, src).then_inc(block_moved["dve"], 1)

            def unload(t, s):
                dve.wait_ge(gram_done, GRAM_STEPS * t + s + 1)
                for j in range(0, 2):
                    last = nc.vector.tensor_copy(*gram_views(t, s, j))
                last.then_inc(gram_moved_dve, 1)

            def pack(t):
                dve.wait_ge(gram_moved_dve, GRAM_STEPS * (t + 1))
                dve.wait_ge(gram_moved_act, GRAM_STEPS * (t + 1))
                nc.vector.transpose(pair_by_b[:, 0:ITEMS * SLOT],
                                    pair_by_n[:, t % 2, :, :].rearrange("n m g -> n (m g)")).then_inc(pairs_by_sample, 1)
                dve.wait_ge(pairs_by_sample, t + 1)
                if t >= 2:
                    dve.wait_ge(block_done, BLOCKS[(PAIRS, t - 2)][0] + 1)
                at = 0
                for repeats, apart, m0, n0, ms, ns in pair_rectangles():
                    first, stride = SLOT * (m0 - 1) + n0, apart * (SLOT + 1)
                    src = pair_by_b[:, first:first + repeats * stride] if repeats > 1 else pair_by_b[:, first:first + SLOT * ms]
                    src = src.rearrange("b (g x) -> b g x", g=repeats)[:, :, 0:min(SLOT * ms, src.shape[1] // repeats)]
                    src = src.rearrange("b g (m n) -> b g m n", m=ms)[:, :, :, 0:ns]
                    size = repeats * ms * ns
                    dst = pairs[:, t % 2, at:at + size].rearrange("b (g m n) -> b g m n", g=repeats, m=ms)
                    last = nc.vector.tensor_copy(dst, src)
                    at += size
                last.then_inc(pairs_packed, 1)

            def layer1(t):
                if t == 0:
                    dve.wait_ge(small_in, 16)
                dve.wait_ge(h1_done, 2 * t + 2)
                for j in range(H1_HALF, H1_CHUNKS):
                    nc.vector.tensor_scalar(h1_t[:, j, :], mlp[1][:, j - H1_HALF, :], b1[:, j:j + 1], 0.0, ALU.add, ALU.max).then_inc(h1_moved[1], 1)

            def layer2(t):
                dve.wait_ge(h2_done, H2_CHUNKS * t + 2)
                nc.vector.tensor_scalar(h2_t[:, 1, :], mlp[1][:, 0, :], b2[:, 1:2], 0.0, ALU.add, ALU.max).then_inc(h2_moved[1], 1)

            def score(t):
                dve.wait_ge(y_done, t + 1)
                nc.vector.tensor_copy(y[:, t:t + 1], mlp[1][:, 1, 0:1]).then_inc(y_moved, 1)

            nc.vector.memset(items_t[:, :, :, :, ITEMS:SLOT].rearrange("d t g j i -> d (t g j) i"), 0.0).then_inc(pads_done, 1)
            nc.vector.memset(pair_by_n[0:P - SLOT, :, PARTNERS, :], 0.0)
            nc.vector.memset(pair_by_n[P - SLOT:P, :, :, :].rearrange("n a m g -> n (a m g)"), 0.0).then_inc(pairs_cleared, 1)
            do = {LOOKUP: one_hot_of, PACK: pack, LAYER1: layer1, LAYER2: layer2, SCORE: score}
            for kind, which in ORDER:
                if kind == TURN:
                    turned_block(*which)
                elif kind == GRAM:
                    unload(*which)
                elif kind in do:
                    do[kind](which)

        @block.scalar
        def _(act):
            def upper_part(k):
                if k >= SPLIT_BUFS:
                    act.wait_ge(block_done, BLOCKS[(LOOKUP, k - SPLIT_BUFS)][0] + 1)
                act.wait_ge(wanted_in[k], 16)
                nc.scalar.activation(wanted_chunk[0:LOOKUP_K, k % 2, :], wanted[0:LOOKUP_K, k % TABLE_BUFS, :], ACT.Identity,
                                     bias=minus_first_row[0:LOOKUP_K, :]).then_inc(chunk_done, 1)
                for h in range(LOOKUP_HALVES):
                    act.wait_ge(table_in[k][h], 32)
                    half = slice(HALF_CHUNKS * h, HALF_CHUNKS * (h + 1))
                    nc.scalar.copy(table_hi[0:LOOKUP_K, k % SPLIT_BUFS, half, :], table[0:LOOKUP_K, k % TABLE_BUFS, half, :]).then_inc(hi_done, 1)

            def looked_up_block(k):
                if k + 1 < LOOKUPS:
                    upper_part(k + 1)
                act.wait_ge(block_done, BLOCKS[(LOOKUP, k)][0] + 1)
                nc.scalar.copy(*looked_up_views(k)).then_inc(block_moved["act"], 1)

            def turned_block(t, q):
                if BLOCKS[(TURN, (t, q))][2] != "act":
                    return
                act.wait_ge(block_done, BLOCKS[(TURN, (t, q))][0] + 1)
                if q == 0:
                    nc.scalar.copy(dense_t[:, t, :], blocks[BLOCKS[(TURN, (t, q))][1]][:, 0, :])
                nc.scalar.copy(*turned_views(t, q)).then_inc(block_moved["act"], 1)

            def unload(t, s):
                if t == 0 and s == 0:
                    act.wait_ge(pairs_cleared, 1)
                if t >= 2 and s == 0:
                    act.wait_ge(pairs_by_sample, t - 1)
                act.wait_ge(gram_done, GRAM_STEPS * t + s + 1)
                for j in range(2, QUADS):
                    last = nc.scalar.copy(*gram_views(t, s, j))
                last.then_inc(gram_moved_act, 1)

            def turned_pairs(t):
                number, bank, _, _ = BLOCKS[(PAIRS, t)]
                act.wait_ge(block_done, number + 1)
                nc.scalar.copy(pairs_t[:, :, :], blocks[bank][0:PAIR_K, 0:PAIR_CHUNKS, :]).then_inc(block_moved["act"], 1)

            def layer1(t):
                if t == 0:
                    act.wait_ge(small_in, 16)
                act.wait_ge(h1_done, 2 * t + 1)
                for j in range(H1_HALF):
                    nc.scalar.activation(h1_t[:, j, :], mlp[0][:, j, :], ACT.Relu, bias=b1[:, j:j + 1]).then_inc(h1_moved[0], 1)

            def layer2(t):
                act.wait_ge(h2_done, H2_CHUNKS * t + 1)
                nc.scalar.activation(h2_t[:, 0, :], mlp[0][:, 0, :], ACT.Relu, bias=b2[:, 0:1]).then_inc(h2_moved[0], 1)

            act.dma_start(index[:, :, :], ids.rearrange("(p t) f -> p t f", t=TILES).bitcast(u32)).then_inc(ids_in, 16)
            act.dma_start(wanted[:, 0, :], ids_by_table[LOOKED_UP[0]:LOOKED_UP[0] + 1, :].to_broadcast([P, BATCH])).then_inc(wanted_in[0], 16)
            act.wait_ge(numbered, 1)
            nc.scalar.activation(minus_first_row[:, :], first_row[:, :], ACT.Identity, scale=-1.0).then_inc(negated, 1)
            act.wait_ge(negated, 1)
            upper_part(0)
            do = {LOOKUP: looked_up_block, PAIRS: turned_pairs, LAYER1: layer1, LAYER2: layer2}
            for kind, which in ORDER:
                if kind == TURN:
                    turned_block(*which)
                elif kind == GRAM:
                    unload(*which)
                elif kind in do:
                    do[kind](which)


def kernel(**inputs):
    import numpy as np
    import concourse.bacc as bacc
    from concourse import mybir
    from concourse.bass_utils import run_bass_kernel_spmd as run

    nc = bacc.Bacc("TRN2", target_bir_lowering=False, num_devices=1)
    arrays = {}

    def put(name, a):
        arrays[name] = a = np.ascontiguousarray(a)
        return nc.dram_tensor(name, a.shape, mybir.dt.from_np(a.dtype), kind="ExternalInput").ap()

    w1 = np.asarray(inputs["W_top1"])
    order = pair_order()
    w1_pairs = np.zeros((PAIR_COLS, H1), w1.dtype)
    for row, (n, m) in enumerate(order):
        if m < ITEMS:
            n, m = sorted(0 if ITEM_TABLE[i] is None else ITEM_TABLE[i] + 1 for i in (n, m))
            w1_pairs[row] = w1[n * ITEMS - n * (n + 1) // 2 + m - n - 1]
    n_pairs = ITEMS * (ITEMS - 1) // 2
    small = np.concatenate([
        np.asarray(inputs["b_top1"]).reshape(H1_CHUNKS, P).T,
        np.asarray(inputs["b_top2"]).reshape(H2_CHUNKS, P).T,
        np.asarray(inputs["W_top3"]).reshape(H2_CHUNKS, P).T,
    ], axis=1)
    ids = np.asarray(inputs["ids"])
    args = [put("ids", ids), put("ids_by_table", ids.T), put("dense", inputs["r_dense"])]
    tables = [put(f"tbl_{f}", inputs[f"tbl_{f}"]) for f in range(TABLES)]
    args += [tables, put("w1_pairs", w1_pairs), put("w1_dense", w1[n_pairs:]), put("w2", inputs["W_top2"]), put("small", small)]
    out = nc.dram_tensor("y_out", (BATCH, 1), mybir.dt.float32, kind="ExternalOutput").ap()
    dlrm_tower(nc, *args, out)
    r = run(nc, [arrays], core_ids=[0])
    return r.results[0]["y_out"]
```

```python
import concourse.bass as bass
from concourse import mybir
from contextlib import ExitStack

P = 128
BATCH = 512
TILES = BATCH // P
TABLES = 26

LOOKED_UP = [2, 9, 10, 11, 12, 13, 14, 16, 19]
LOOKUPS = len(LOOKED_UP)
LOOKUP_FROM = [0] * (LOOKUPS - 1) + [2]
LOOKUP_ROWS = 1000
LOOKUP_CHUNKS = 8
LOOKUP_K = LOOKUP_ROWS // LOOKUP_CHUNKS
LOOKUP_SPRAY = 112
GATHERED = [f for f in range(TABLES) if f not in LOOKED_UP]

ITEM_TABLE = [None] + GATHERED + LOOKED_UP[::-1]
ITEMS = len(ITEM_TABLE)
TURNED_ITEMS = [1 + len(GATHERED) + sum(t < first for first in LOOKUP_FROM) for t in range(TILES)]
SLOT = 32
QUADS = P // SLOT
GROUPS = P // QUADS
ITEM_GROUP = 4
ITEM_GROUPS = -(-max(TURNED_ITEMS) // ITEM_GROUP)
PARTNERS = ITEMS - 1
STATIONARY = (QUADS - 1) * SLOT + ITEMS - 1
GROUPS_PER_BANK = 4
GRAM_BANKS = 2
GRAM_STEPS = GROUPS // (GROUPS_PER_BANK * GRAM_BANKS)
SQUARE = 14
PAIR_COLS = 378
PAIR_CHUNKS = 3
PAIR_K = PAIR_COLS // PAIR_CHUNKS
H1, H2 = 512, 256
H1_CHUNKS, H2_CHUNKS = H1 // P, H2 // P
H1_HALF = H1_CHUNKS // 2
TABLE_BUFS = 3
SPLIT_BUFS = 2
LOOKUP_HALVES = 2
HALF_CHUNKS = LOOKUP_CHUNKS // LOOKUP_HALVES
WARM_UP = 11

LOOKUP = "lookup"
TURN = "turn"
GRAM = "gram"
PACK = "pack"
PAIRS = "pairs"
LAYER1 = "layer1"
LAYER2, SCORE = "layer2", "score"


def step_order():
    turns = iter([(TURN, (t, q)) for t in range(TILES) for q in range(ITEM_GROUPS)])
    order = []
    for k in range(LOOKUPS):
        order.append((LOOKUP, k))
        if k < LOOKUPS - 1:
            order.append(next(turns))

    def turn():
        order.append(next(turns))

    def gram(t, s):
        order.append((GRAM, (t, s)))

    def step(kind, t):
        order.append((kind, t))

    def layer1(t, halves=(0, 1)):
        order.extend((LAYER1, (t, half)) for half in halves)

    gram(0, 0), gram(0, 1), turn(), gram(0, 2), turn(), gram(0, 3), step(PACK, 0)
    gram(1, 0), gram(1, 1), turn(), step(PAIRS, 0), gram(1, 2), turn()
    gram(1, 3), turn(), step(PACK, 1), layer1(0), turn(), step(LAYER2, 0), turn(), step(PAIRS, 1), step(SCORE, 0)
    gram(2, 0), gram(2, 1), turn(), gram(2, 2), layer1(1), turn()
    gram(2, 3), turn(), step(PACK, 2), step(LAYER2, 1), step(PAIRS, 2), layer1(2, [0]), turn(), turn(), step(SCORE, 1)
    gram(3, 0), gram(3, 1), gram(3, 2), gram(3, 3), step(PACK, 3)
    layer1(2, [1]), step(LAYER2, 2), step(PAIRS, 3), step(SCORE, 2)
    layer1(3), step(LAYER2, 3), step(SCORE, 3)
    assert next(turns, None) is None
    return order


ORDER = step_order()


def block_owners():
    owners, counts = {}, {"act": 0, "dve": 0}
    first_gram = ORDER.index((GRAM, (0, 0)))
    for at, step in enumerate(ORDER):
        if step[0] not in (LOOKUP, TURN, PAIRS):
            continue
        late = step[0] == TURN and step[1][0] >= 2
        engine = "dve" if late and step[1][1] % 2 else "act"
        counts[engine] += 1
        bank = len(owners) % (BLOCK_BANKS if at < first_gram else 2)
        owners[step] = (len(owners), bank, engine, counts[engine])
    return owners


BLOCK_BANKS = 4
RECTANGLE_REACH = 8


def layer_engine(t, chunk):
    return "dve" if t == TILES - 1 and chunk % 2 else "act"


def h1_ready(t, j):
    return H1_CHUNKS * t + (j + 1 if t == TILES - 1 else H1_HALF * (j // H1_HALF + 1))


BLOCKS = block_owners()


def bank_before(step):
    number, bank, _, _ = BLOCKS[step]
    before = [s for s in BLOCKS if BLOCKS[s][0] < number and BLOCKS[s][1] == bank]
    return before[-1] if before else None


def pair_rectangles():
    return [
        (1, 28, SQUARE, 0, SQUARE, SQUARE),
        (2, 14, 7, 0, 7, 7),
        (4, 7, 3, 0, 4, 3),
        (4, 7, 1, 0, 1, 1),
        (4, 7, 2, 0, 1, 2),
        (4, 7, 5, 3, 2, 2),
        (4, 7, 4, 3, 1, 1),
        (4, 7, 6, 5, 1, 1),
    ]


def pair_order():
    return [
        (g * apart + n0 + n, g * apart + m0 + m)
        for repeats, apart, m0, n0, ms, ns in pair_rectangles()
        for g in range(repeats)
        for m in range(ms)
        for n in range(ns)
    ]


def dlrm_tower(nc, ids, ids_by_table, dense, tables, w1_pairs, w1_dense, w2, small, out):
    f32 = mybir.dt.float32
    f32r = mybir.dt.float32r
    i32 = mybir.dt.int32
    u32 = mybir.dt.uint32
    ALU = mybir.AluOpType
    ACT = mybir.ActivationFunctionType

    with ExitStack() as ctx:
        def sb(name, shape, dt=f32):
            return ctx.enter_context(nc.sbuf_tensor(name, shape, dt))

        def ps(name, shape):
            return ctx.enter_context(nc.psum_tensor(name, shape, f32))

        def sem(name):
            return ctx.enter_context(nc.semaphore(name))

        index = sb("index", [P, TILES, TABLES], u32)
        rows = sb("rows", [P, TILES, max(TURNED_ITEMS), P])
        wanted = sb("wanted", [P, TABLE_BUFS, BATCH], i32)
        table = sb("table", [P, TABLE_BUFS, LOOKUP_CHUNKS, P])
        table_hi = sb("table_hi", [P, SPLIT_BUFS, LOOKUP_CHUNKS, P], f32r)
        table_lo = sb("table_lo", [P, SPLIT_BUFS, LOOKUP_CHUNKS, P], f32r)
        one_hot = sb("one_hot", [P, 2, LOOKUP_CHUNKS, BATCH], f32r)
        first_row = sb("first_row", [P, 1])
        minus_first_row = sb("minus_first_row", [P, 1])
        wanted_chunk = sb("wanted_chunk", [P, 2, BATCH])
        ident = sb("ident", [P, P])
        zeros = sb("zeros", [P, P])
        items_t = sb("items_t", [P, TILES, GROUPS, QUADS, SLOT])
        dense_t = sb("dense_t", [P, TILES, P])
        pair_by_n = sb("pair_by_n", [P, 2, ITEMS, GROUPS])
        pair_by_b = sb("pair_by_b", [P, (ITEMS + RECTANGLE_REACH) * SLOT])
        pairs = sb("pairs", [P, 2, PAIR_COLS])
        pairs_t = sb("pairs_t", [PAIR_K, PAIR_CHUNKS, P])
        h1_t = sb("h1_t", [P, H1_CHUNKS, P])
        h2_t = sb("h2_t", [P, H2_CHUNKS, P])
        y = sb("y", [P, TILES])
        w1p = sb("w1p", [PAIR_K, PAIR_CHUNKS, H1])
        w1d = sb("w1d", [P, H1])
        w2s = sb("w2s", [P, H1_CHUNKS, H2])
        smalls = sb("smalls", [P, H1_CHUNKS + 2 * H2_CHUNKS])
        b1 = smalls[:, 0:H1_CHUNKS]
        b2 = smalls[:, H1_CHUNKS:H1_CHUNKS + H2_CHUNKS]
        w3 = smalls[:, H1_CHUNKS + H2_CHUNKS:H1_CHUNKS + 2 * H2_CHUNKS]

        blocks = [ps(f"block{i}", [P, ITEM_GROUP, P]) for i in range(BLOCK_BANKS)]
        gram = [ps(f"gram{i}", [P, GRAM_BANKS, 512]) for i in range(2)]
        mlp = blocks[2:4]

        def h1_place(t, j):
            side, k = j // H1_HALF, j % H1_HALF
            if t < TILES - 1:
                return mlp[side][:, k, :], True
            return (mlp[side][:, 0, :], gram[0][:, side, 0:P])[k], False

        ids_in = sem("ids_in")
        dense_in = sem("dense_in")
        wanted_in = [sem(f"wanted_in{k}") for k in range(LOOKUPS)]
        table_in = [[sem(f"table_in{k}_{h}") for h in range(LOOKUP_HALVES)] for k in range(LOOKUPS)]
        numbered = sem("numbered")
        negated = sem("negated")
        hi_done = sem("hi_done")
        lo_done = sem("lo_done")
        chunk_done = sem("chunk_done")
        one_hot_done = sem("one_hot_done")
        w1_in = sem("w1_in")
        w2_in = sem("w2_in")
        small_in = sem("small_in")
        rows_in = [[sem(f"rows_in{t}_{q}") for q in range(ITEM_GROUPS)] for t in range(TILES)]
        zeros_done = sem("zeros_done")
        ident_zero = sem("ident_zero")
        ident_done = sem("ident_done")
        pads_done = sem("pads_done")
        pairs_cleared = sem("pairs_cleared")
        block_done = sem("block_done")
        block_moved = {"act": sem("block_moved_act"), "dve": sem("block_moved_dve")}
        gram_done = sem("gram_done")
        gram_moved_dve = sem("gram_moved_dve")
        gram_moved_act = sem("gram_moved_act")
        upper_by_sample = sem("upper_by_sample")
        pairs_by_sample = sem("pairs_by_sample")
        square_packed = sem("square_packed")
        pairs_packed = sem("pairs_packed")
        h1_done = sem("h1_done")
        h1_moved = [sem(f"h1_moved{j}") for j in range(H1_CHUNKS)]
        h2_done = sem("h2_done")
        h2_moved = [sem("h2_moved_half0"), sem("h2_moved_half1")]
        y_done = sem("y_done")
        y_moved = sem("y_moved")
        out_done = sem("out_done")

        def group_items(t, q):
            return range(ITEM_GROUP * q, min(ITEM_GROUP * (q + 1), TURNED_ITEMS[t]))

        def lookup_samples(k):
            return P * (TILES - LOOKUP_FROM[k])

        block = ctx.enter_context(nc.Block())

        @block.sync
        def _(sp):
            for k, f in enumerate(LOOKED_UP):
                if k >= TABLE_BUFS:
                    sp.wait_ge(chunk_done, k - TABLE_BUFS + 1)
                    sp.wait_ge(hi_done, LOOKUP_HALVES * (k - TABLE_BUFS + 1))
                    sp.wait_ge(lo_done, LOOKUP_HALVES * (k - TABLE_BUFS + 1))
                sp.dma_start(wanted[:, k % TABLE_BUFS, :], ids_by_table[f:f + 1, :].to_broadcast([P, BATCH])).then_inc(wanted_in[k], 16)
                src = tables[f].rearrange("(k c) d -> k c d", c=LOOKUP_CHUNKS)
                for h in range(LOOKUP_HALVES):
                    half = slice(HALF_CHUNKS * h, HALF_CHUNKS * (h + 1))
                    for part in (slice(0, LOOKUP_SPRAY), slice(LOOKUP_SPRAY, LOOKUP_K)):
                        sp.dma_start(table[part, k % TABLE_BUFS, half, :], src[part, half, :]).then_inc(table_in[k][h], 16)
                if k == 0:
                    sp.dma_start(rows[:, :, 0, :], dense.rearrange("(p t) d -> p t d", t=TILES)).then_inc(dense_in, 16)
            sp.dma_start(w1p[:, :, :], w1_pairs.rearrange("(c k) n -> k c n", k=PAIR_K)).then_inc(w1_in, 16)
            sp.dma_start(w1d[:, :], w1_dense).then_inc(w1_in, 16)
            sp.dma_start(w2s[:, :, :], w2.rearrange("(c k) n -> k c n", k=P)).then_inc(w2_in, 16)
            sp.dma_start(smalls[:, :], small).then_inc(small_in, 16)
            sp.wait_ge(y_moved, TILES)
            sp.dma_start(out.rearrange("(p t) o -> p (t o)", t=TILES), y[:, :]).then_inc(out_done, 16)
            sp.wait_ge(out_done, 16)

        @block.gpsimd
        def _(pool):
            nc.gpsimd.iota(first_row[:, :], pattern=[[0, 1]], base=0, channel_multiplier=LOOKUP_CHUNKS,
                           allow_small_or_imprecise_dtypes=True).then_inc(numbered, 1)
            nc.gpsimd.memset(zeros[:, :], 0.0).then_inc(zeros_done, 1)
            nc.gpsimd.memset(ident[:, :], 0.0).then_inc(ident_zero, 1)
            pool.wait_ge(ident_zero, 1)
            nc.gpsimd.affine_select(out=ident[:, :], in_=ident[:, :], compare_op=ALU.not_equal, fill=1.0, base=0,
                                    pattern=[[-1, P]], channel_multiplier=1).then_inc(ident_done, 1)
            nc.gpsimd.memset(pair_by_n[:, :, :, :].rearrange("n a m g -> n (a m g)"), 0.0).then_inc(pairs_cleared, 1)
            pool.wait_ge(ids_in, 16)
            for t in range(TILES):
                for q in range(ITEM_GROUPS):
                    for i in group_items(t, q):
                        if i == 0:
                            continue
                        pool.indirect_dma_start(
                            rows[:, t, i, :], None, tables[ITEM_TABLE[i]][:, :],
                            bass.IndirectOffsetOnAxis(ap=index[:, t, ITEM_TABLE[i]:ITEM_TABLE[i] + 1], axis=0),
                        ).then_inc(rows_in[t][q], 16)

        @block.tensor
        def _(pe):
            def bank_free(step):
                before = bank_before(step)
                if before:
                    _, _, engine, count = BLOCKS[before]
                    pe.wait_ge(block_moved[engine], count)
                return blocks[BLOCKS[step][1]]

            def lookup(k):
                samples = lookup_samples(k)
                out_d = bank_free((LOOKUP, k))[:, :, :].rearrange("d i b -> d (i b)")[:, 0:samples]
                for h in range(LOOKUP_HALVES):
                    for part, part_done in ((table_hi, hi_done), (table_lo, lo_done)):
                        pe.wait_ge(part_done, LOOKUP_HALVES * k + h + 1)
                        for c in range(HALF_CHUNKS * h, HALF_CHUNKS * (h + 1)):
                            if part is table_hi:
                                pe.wait_ge(one_hot_done, LOOKUP_CHUNKS * k + c + 1)
                            last = nc.tensor.matmul(out_d, part[0:LOOKUP_K, k % SPLIT_BUFS, c, :], one_hot[0:LOOKUP_K, k % 2, c, 0:samples],
                                                    start=(part is table_hi and c == 0),
                                                    stop=(part is table_lo and c == LOOKUP_CHUNKS - 1))
                last.then_inc(block_done, 1)

            def turn(t, q):
                gathered = len([i for i in group_items(t, q) if i > 0])
                bank = bank_free((TURN, (t, q)))
                pe.wait_ge(rows_in[t][q], 16 * gathered)
                if t == 0 and q == 0:
                    pe.wait_ge(ident_done, 1)
                    pe.wait_ge(dense_in, 16)
                for k, i in enumerate(group_items(t, q)):
                    last = nc.tensor.transpose(bank[:, k, :], rows[:, t, i, :], ident[:, :])
                last.then_inc(block_done, 1)

            def products(t, s):
                if s == 0:
                    needed = [(TURN, (t, q)) for q in range(ITEM_GROUPS)] + [(LOOKUP, k) for k in range(LOOKUPS)]
                    needed = [x for x in needed if x[0] == TURN or LOOKUP_FROM[x[1]] <= t]
                    for name in ("act", "dve"):
                        counts = [BLOCKS[x][3] for x in needed if BLOCKS[x][2] == name]
                        if counts:
                            pe.wait_ge(block_moved[name], max(counts))
                    if t == 0:
                        pe.wait_ge(pads_done, 1)
                step = GRAM_STEPS * t + s
                if step >= 2:
                    pe.wait_ge(gram_moved_dve, step - 1)
                    pe.wait_ge(gram_moved_act, step - 1)
                cols = QUADS * PARTNERS
                for bank in range(GRAM_BANKS):
                    for k in range(GROUPS_PER_BANK):
                        samples = items_t[:, t, (s * GRAM_BANKS + bank) * GROUPS_PER_BANK + k, :, :]
                        last = nc.tensor.matmul(gram[step % 2][0:STATIONARY, bank, cols * k:cols * (k + 1)],
                                                samples.rearrange("d j i -> d (j i)")[:, 0:STATIONARY], samples[:, :, 1:ITEMS],
                                                start=True, stop=True)
                last.then_inc(gram_done, 1)

            def turn_pairs(t):
                bank = bank_free((PAIRS, t))
                pe.wait_ge(square_packed, t + 1)
                for c in range(PAIR_CHUNKS):
                    if PAIR_K * (c + 1) > SQUARE * SQUARE:
                        pe.wait_ge(pairs_packed, t + 1)
                    last = nc.tensor.transpose(bank[0:PAIR_K, c, :], pairs[:, t % 2, PAIR_K * c:PAIR_K * (c + 1)], ident[:, :])
                last.then_inc(block_done, 1)

            def layer1(t, side):
                if t == 0 and side == 0:
                    pe.wait_ge(w1_in, 32)
                if t > 0:
                    pe.wait_ge(*[(h2_moved[0], t), (y_moved, t)][side])
                chunks = range(side * H1_HALF, (side + 1) * H1_HALF)
                for j in chunks:
                    place, shared = h1_place(t, j)
                    nc.tensor.matmul(place, w1d[:, P * j:P * (j + 1)], dense_t[:, t, :], start=(j == chunks[0] or not shared), stop=False)
                _, _, engine, count = BLOCKS[(PAIRS, t)]
                pe.wait_ge(block_moved[engine], count)
                for j in chunks:
                    place, shared = h1_place(t, j)
                    for c in range(PAIR_CHUNKS):
                        last = nc.tensor.matmul(place, w1p[:, c, P * j:P * (j + 1)], pairs_t[:, c, :], start=False,
                                                stop=(c == PAIR_CHUNKS - 1 and (j == chunks[-1] or not shared)))
                    last.then_inc(h1_done, 1)

            def layer2(t):
                if t == 0:
                    pe.wait_ge(w2_in, 16)
                if h1_place(t, 0)[1]:
                    pe.wait_ge(h1_moved[1], t + 1)
                for j in range(H2_CHUNKS):
                    for c in range(H1_CHUNKS):
                        if j == 0:
                            pe.wait_ge(h1_moved[c], t + 1)
                        last = nc.tensor.matmul(mlp[j][:, 0, :], w2s[:, c, P * j:P * (j + 1)], h1_t[:, c, :],
                                                start=(c == 0), stop=(c == H1_CHUNKS - 1))
                    last.then_inc(h2_done, 1)

            def score(t):
                if t == 0:
                    pe.wait_ge(small_in, 16)
                for c in range(H2_CHUNKS):
                    pe.wait_ge(h2_moved[1 - c], t + 1)
                    last = nc.tensor.matmul(mlp[1][:, 1, 0:1], h2_t[:, 1 - c, :], w3[:, 1 - c:2 - c],
                                            start=(c == 0), stop=(c == H2_CHUNKS - 1))
                last.then_inc(y_done, 1)

            pe.wait_ge(zeros_done, 1)
            for _ in range(WARM_UP):
                nc.tensor.matmul(gram[0][:, 0, 0:P], zeros[:, :], zeros[:, :], start=True, stop=True)
            do = {LOOKUP: lookup, PAIRS: turn_pairs, LAYER2: layer2, SCORE: score}
            for kind, which in ORDER:
                if kind == TURN:
                    turn(*which)
                elif kind == GRAM:
                    products(*which)
                elif kind == LAYER1:
                    layer1(*which)
                elif kind in do:
                    do[kind](which)

        def looked_up_views(k):
            src = blocks[BLOCKS[(LOOKUP, k)][1]][:, :, :].rearrange("d i b -> d (i b)")[:, 0:lookup_samples(k)]
            src = src.rearrange("d (j g t) -> d j g t", j=QUADS, g=GROUPS)
            return items_t[:, LOOKUP_FROM[k]:, :, :, ITEMS - 1 - k].rearrange("d t g j -> d j g t"), src

        def turned_views(t, q):
            lo, hi = group_items(t, q)[0], group_items(t, q)[-1] + 1
            src = blocks[BLOCKS[(TURN, (t, q))][1]][:, 0:hi - lo, :].rearrange("d i (j g) -> d i j g", j=QUADS)
            return items_t[:, t, :, :, lo:hi].rearrange("d g j i -> d i j g"), src

        def gram_views(t, s, j):
            cols = QUADS * PARTNERS
            part = slice(SLOT * j, min(SLOT * (j + 1), STATIONARY))
            src = gram[(GRAM_STEPS * t + s) % 2][part, :, 0:GROUPS_PER_BANK * cols]
            src = src.rearrange("n b (k j m) -> n b k j m", j=QUADS, m=PARTNERS)[:, :, :, j, :]
            per_step = GRAM_BANKS * GROUPS_PER_BANK
            dst = pair_by_n[part, t % 2, 0:PARTNERS, per_step * s:per_step * (s + 1)]
            dst = dst.rearrange("n m (b k) -> n b k m", k=GROUPS_PER_BANK)
            return dst, src

        def rectangle_views(t, n):
            at = sum(x[0] * x[4] * x[5] for x in pair_rectangles()[:n])
            repeats, apart, m0, n0, ms, ns = pair_rectangles()[n]
            first, stride = SLOT * (m0 - 1) + n0, apart * (SLOT + 1)
            src = pair_by_b[:, first:first + (repeats * stride if repeats > 1 else SLOT * ms)]
            src = src.rearrange("b (g x) -> b g x", g=repeats)[:, :, 0:min(SLOT * ms, src.shape[1] // repeats)]
            src = src.rearrange("b g (m n) -> b g m n", m=ms)[:, :, :, 0:ns]
            dst = pairs[:, t % 2, at:at + repeats * ms * ns].rearrange("b (g m n) -> b g m n", g=repeats, m=ms)
            return dst, src

        @block.vector
        def _(dve):
            def one_hot_of(k):
                if k >= 2:
                    dve.wait_ge(block_done, BLOCKS[(LOOKUP, k - 2)][0] + 1)
                for c in range(LOOKUP_CHUNKS):
                    if c % HALF_CHUNKS == 1:
                        half = slice(c - 1, c - 1 + HALF_CHUNKS)
                        dve.wait_ge(table_in[k][c // HALF_CHUNKS], 32)
                        dve.wait_ge(hi_done, LOOKUP_HALVES * k + c // HALF_CHUNKS + 1)
                        nc.vector.tensor_tensor(table_lo[0:LOOKUP_K, k % SPLIT_BUFS, half, :], table[0:LOOKUP_K, k % TABLE_BUFS, half, :],
                                                table_hi[0:LOOKUP_K, k % SPLIT_BUFS, half, :].bitcast(f32), ALU.subtract).then_inc(lo_done, 1)
                    if c == 0:
                        dve.wait_ge(chunk_done, k + 1)
                    samples = wanted_chunk[0:LOOKUP_K, k % 2, :].rearrange("r (p t) -> r p t", t=TILES)[:, :, LOOKUP_FROM[k]:]
                    hot = one_hot[0:LOOKUP_K, k % 2, c, 0:lookup_samples(k)].rearrange("r (p t) -> r p t", p=P)
                    nc.vector.tensor_scalar(hot, samples, float(c), None, ALU.is_equal).then_inc(one_hot_done, 1)

            def turned_block(t, q):
                if BLOCKS[(TURN, (t, q))][2] != "dve":
                    return
                dve.wait_ge(block_done, BLOCKS[(TURN, (t, q))][0] + 1)
                dst, src = turned_views(t, q)
                if q == 0:
                    nc.vector.tensor_copy(dense_t[:, t, :], blocks[BLOCKS[(TURN, (t, q))][1]][:, 0, :])
                nc.vector.tensor_copy(dst, src).then_inc(block_moved["dve"], 1)

            def unload(t, s):
                if t == 0 and s == 0:
                    dve.wait_ge(pairs_cleared, 1)
                dve.wait_ge(gram_done, GRAM_STEPS * t + s + 1)
                for j in range(0, 2):
                    last = nc.vector.tensor_copy(*gram_views(t, s, j))
                last.then_inc(gram_moved_dve, 1)

            def pack(t):
                dve.wait_ge(gram_moved_dve, GRAM_STEPS * (t + 1))
                dve.wait_ge(gram_moved_act, GRAM_STEPS * (t + 1))
                if t:
                    dve.wait_ge(square_packed, t)
                for part, done in ((slice(SQUARE - 1, ITEMS), upper_by_sample), (slice(0, SQUARE - 1), pairs_by_sample)):
                    nc.vector.transpose(pair_by_b[:, SLOT * part.start:SLOT * part.stop],
                                        pair_by_n[:, t % 2, part, :].rearrange("n m g -> n (m g)")).then_inc(done, 1)
                dve.wait_ge(upper_by_sample, t + 1)
                dve.wait_ge(pairs_by_sample, t + 1)
                if t >= 2:
                    dve.wait_ge(block_done, BLOCKS[(PAIRS, t - 2)][0] + 1)
                for n in range(1, len(pair_rectangles())):
                    last = nc.vector.tensor_copy(*rectangle_views(t, n))
                last.then_inc(pairs_packed, 1)

            def layer1(t, side):
                for j in range(side * H1_HALF, (side + 1) * H1_HALF):
                    if layer_engine(t, j) == "dve":
                        dve.wait_ge(small_in, 16)
                        dve.wait_ge(h1_done, h1_ready(t, j))
                        nc.vector.tensor_scalar(h1_t[:, j, :], h1_place(t, j)[0], b1[:, j:j + 1], 0.0, ALU.add, ALU.max).then_inc(h1_moved[j], 1)

            def layer2(t):
                for half in range(2):
                    if layer_engine(t, half) == "dve":
                        dve.wait_ge(h2_done, H2_CHUNKS * t + half + 1)
                        nc.vector.tensor_scalar(h2_t[:, half, :], mlp[half][:, 0, :], b2[:, half:half + 1], 0.0, ALU.add, ALU.max).then_inc(h2_moved[half], 1)

            def score(t):
                if layer_engine(t, 1) == "dve":
                    dve.wait_ge(y_done, t + 1)
                    nc.vector.tensor_copy(y[:, t:t + 1], mlp[1][:, 1, 0:1]).then_inc(y_moved, 1)

            nc.vector.memset(items_t[:, :, :, :, ITEMS:SLOT].rearrange("d t g j i -> d (t g j) i"), 0.0).then_inc(pads_done, 1)
            do = {LOOKUP: one_hot_of, PACK: pack, LAYER2: layer2, SCORE: score}
            for kind, which in ORDER:
                if kind == TURN:
                    turned_block(*which)
                elif kind == GRAM:
                    unload(*which)
                elif kind == LAYER1:
                    layer1(*which)
                elif kind in do:
                    do[kind](which)

        @block.scalar
        def _(act):
            def upper_part(k):
                if k >= SPLIT_BUFS:
                    act.wait_ge(block_done, BLOCKS[(LOOKUP, k - SPLIT_BUFS)][0] + 1)
                act.wait_ge(wanted_in[k], 16)
                nc.scalar.activation(wanted_chunk[0:LOOKUP_K, k % 2, :], wanted[0:LOOKUP_K, k % TABLE_BUFS, :], ACT.Identity,
                                     bias=minus_first_row[0:LOOKUP_K, :]).then_inc(chunk_done, 1)
                for h in range(LOOKUP_HALVES):
                    act.wait_ge(table_in[k][h], 32)
                    half = slice(HALF_CHUNKS * h, HALF_CHUNKS * (h + 1))
                    nc.scalar.copy(table_hi[0:LOOKUP_K, k % SPLIT_BUFS, half, :], table[0:LOOKUP_K, k % TABLE_BUFS, half, :]).then_inc(hi_done, 1)

            def looked_up_block(k):
                if k + 1 < LOOKUPS:
                    upper_part(k + 1)
                act.wait_ge(block_done, BLOCKS[(LOOKUP, k)][0] + 1)
                nc.scalar.copy(*looked_up_views(k)).then_inc(block_moved["act"], 1)

            def turned_block(t, q):
                if BLOCKS[(TURN, (t, q))][2] != "act":
                    return
                act.wait_ge(block_done, BLOCKS[(TURN, (t, q))][0] + 1)
                if q == 0:
                    nc.scalar.copy(dense_t[:, t, :], blocks[BLOCKS[(TURN, (t, q))][1]][:, 0, :])
                nc.scalar.copy(*turned_views(t, q)).then_inc(block_moved["act"], 1)

            def unload(t, s):
                if t == 0 and s == 0:
                    act.wait_ge(pairs_cleared, 1)
                if t >= 2 and s == 0:
                    act.wait_ge(pairs_by_sample, t - 1)
                act.wait_ge(gram_done, GRAM_STEPS * t + s + 1)
                for j in range(2, QUADS):
                    last = nc.scalar.copy(*gram_views(t, s, j))
                last.then_inc(gram_moved_act, 1)

            def pack_square(t):
                act.wait_ge(upper_by_sample, t + 1)
                if t >= 2:
                    act.wait_ge(block_done, BLOCKS[(PAIRS, t - 2)][0] + 1)
                nc.scalar.copy(*rectangle_views(t, 0)).then_inc(square_packed, 1)

            def turned_pairs(t):
                number, bank, _, _ = BLOCKS[(PAIRS, t)]
                act.wait_ge(block_done, number + 1)
                nc.scalar.copy(pairs_t[:, :, :], blocks[bank][0:PAIR_K, 0:PAIR_CHUNKS, :]).then_inc(block_moved["act"], 1)

            def layer1(t, side):
                for j in range(side * H1_HALF, (side + 1) * H1_HALF):
                    if layer_engine(t, j) == "act":
                        act.wait_ge(small_in, 16)
                        act.wait_ge(h1_done, h1_ready(t, j))
                        nc.scalar.activation(h1_t[:, j, :], h1_place(t, j)[0], ACT.Relu, bias=b1[:, j:j + 1]).then_inc(h1_moved[j], 1)

            def layer2(t):
                for half in range(2):
                    if layer_engine(t, half) == "act":
                        act.wait_ge(h2_done, H2_CHUNKS * t + half + 1)
                        nc.scalar.activation(h2_t[:, half, :], mlp[half][:, 0, :], ACT.Relu, bias=b2[:, half:half + 1]).then_inc(h2_moved[half], 1)

            def score(t):
                if layer_engine(t, 1) == "act":
                    act.wait_ge(y_done, t + 1)
                    nc.scalar.copy(y[:, t:t + 1], mlp[1][:, 1, 0:1]).then_inc(y_moved, 1)

            act.dma_start(index[:, :, :], ids.rearrange("(p t) f -> p t f", t=TILES).bitcast(u32)).then_inc(ids_in, 16)
            act.wait_ge(numbered, 1)
            nc.scalar.activation(minus_first_row[:, :], first_row[:, :], ACT.Identity, scale=-1.0).then_inc(negated, 1)
            act.wait_ge(negated, 1)
            upper_part(0)
            do = {LOOKUP: looked_up_block, PACK: pack_square, PAIRS: turned_pairs, LAYER2: layer2, SCORE: score}
            for kind, which in ORDER:
                if kind == TURN:
                    turned_block(*which)
                elif kind == GRAM:
                    unload(*which)
                elif kind == LAYER1:
                    layer1(*which)
                elif kind in do:
                    do[kind](which)


def kernel(**inputs):
    import numpy as np
    import concourse.bacc as bacc
    from concourse import mybir
    from concourse.bass_utils import run_bass_kernel_spmd as run

    nc = bacc.Bacc("TRN2", target_bir_lowering=False, num_devices=1)
    arrays = {}

    def put(name, a):
        arrays[name] = a = np.ascontiguousarray(a)
        return nc.dram_tensor(name, a.shape, mybir.dt.from_np(a.dtype), kind="ExternalInput").ap()

    w1 = np.asarray(inputs["W_top1"])
    order = pair_order()
    w1_pairs = np.zeros((PAIR_COLS, H1), w1.dtype)
    for row, (n, m) in enumerate(order):
        if m < ITEMS:
            n, m = sorted(0 if ITEM_TABLE[i] is None else ITEM_TABLE[i] + 1 for i in (n, m))
            w1_pairs[row] = w1[n * ITEMS - n * (n + 1) // 2 + m - n - 1]
    n_pairs = ITEMS * (ITEMS - 1) // 2
    small = np.concatenate([
        np.asarray(inputs["b_top1"]).reshape(H1_CHUNKS, P).T,
        np.asarray(inputs["b_top2"]).reshape(H2_CHUNKS, P).T,
        np.asarray(inputs["W_top3"]).reshape(H2_CHUNKS, P).T,
    ], axis=1)
    ids = np.asarray(inputs["ids"])
    args = [put("ids", ids), put("ids_by_table", ids.T), put("dense", inputs["r_dense"])]
    tables = [put(f"tbl_{f}", inputs[f"tbl_{f}"]) for f in range(TABLES)]
    args += [tables, put("w1_pairs", w1_pairs), put("w1_dense", w1[n_pairs:]), put("w2", inputs["W_top2"]), put("small", small)]
    out = nc.dram_tensor("y_out", (BATCH, 1), mybir.dt.float32, kind="ExternalOutput").ap()
    dlrm_tower(nc, *args, out)
    r = run(nc, [arrays], core_ids=[0])
    return r.results[0]["y_out"]
```
